# Optimizing a Trainium2 kernel written in Bass

```python
import numpy as np
import jax
import jax.numpy as jnp

def _softmax(x, axis=-1):
    return jax.nn.softmax(x, axis=axis)

def _gelu(x):
    return jax.nn.gelu(x, approximate=True)

def _silu(x):
    return jax.nn.silu(x)

def _sigmoid(x):
    return jax.nn.sigmoid(x)

def _layernorm(x, axis=-1, eps=1e-05):
    m = jnp.mean(x, axis=axis, keepdims=True)
    v = jnp.var(x, axis=axis, keepdims=True)
    return (x - m) / jnp.sqrt(v + eps)

def _scatter_add(tgt, idx, src, axis=0):
    return tgt.at[idx].add(src)

def _segment_sum(src, seg, n):
    return jax.ops.segment_sum(src, seg, n)
kernel_name = 'mk_dlrm_tower_d1_rec_r8_766735'

def setup_inputs(seed: int=0):
    np.random.seed(seed)
    _w = jnp.asarray

    def _rec_inputs():
        import jax
        import jax.numpy as jnp
        _tk = jax.random.key(seed)
        ids = jnp.stack([jax.random.randint(jax.random.fold_in(_tk, 200 + f), (512,), 0, v, jnp.int32) for f, v in enumerate([12500, 125000, 1250, 12500, 1000, 1000, 1000, 12500, 12500, 1250, 12500, 1250, 1000, 1250, 1250, 1250, 1000, 12500, 1250, 12500, 12500, 1250, 1250, 1000, 1250, 1250])], axis=1)
        tbl_0 = 0.05 * jax.random.normal(jax.random.fold_in(_tk, 500 + 0), (12500, 128), jnp.float32)
        tbl_1 = 0.05 * jax.random.normal(jax.random.fold_in(_tk, 500 + 1), (125000, 128), jnp.float32)
        tbl_2 = 0.05 * jax.random.normal(jax.random.fold_in(_tk, 500 + 2), (1250, 128), jnp.float32)
        tbl_3 = 0.05 * jax.random.normal(jax.random.fold_in(_tk, 500 + 3), (12500, 128), jnp.float32)
        tbl_4 = 0.05 * jax.random.normal(jax.random.fold_in(_tk, 500 + 4), (1000, 128), jnp.float32)
        tbl_5 = 0.05 * jax.random.normal(jax.random.fold_in(_tk, 500 + 5), (1000, 128), jnp.float32)
        tbl_6 = 0.05 * jax.random.normal(jax.random.fold_in(_tk, 500 + 6), (1000, 128), jnp.float32)
        tbl_7 = 0.05 * jax.random.normal(jax.random.fold_in(_tk, 500 + 7), (12500, 128), jnp.float32)
        tbl_8 = 0.05 * jax.random.normal(jax.random.fold_in(_tk, 500 + 8), (12500, 128), jnp.float32)
        tbl_9 = 0.05 * jax.random.normal(jax.random.fold_in(_tk, 500 + 9), (1250, 128), jnp.float32)
        tbl_10 = 0.05 * jax.random.normal(jax.random.fold_in(_tk, 500 + 10), (12500, 128), jnp.float32)
        tbl_11 = 0.05 * jax.random.normal(jax.random.fold_in(_tk, 500 + 11), (1250, 128), jnp.float32)
        tbl_12 = 0.05 * jax.random.normal(jax.random.fold_in(_tk, 500 + 12), (1000, 128), jnp.float32)
        tbl_13 = 0.05 * jax.random.normal(jax.random.fold_in(_tk, 500 + 13), (1250, 128), jnp.float32)
        tbl_14 = 0.05 * jax.random.normal(jax.random.fold_in(_tk, 500 + 14), (1250, 128), jnp.float32)
        tbl_15 = 0.05 * jax.random.normal(jax.random.fold_in(_tk, 500 + 15), (1250, 128), jnp.float32)
        tbl_16 = 0.05 * jax.random.normal(jax.random.fold_in(_tk, 500 + 16), (1000, 128), jnp.float32)
        tbl_17 = 0.05 * jax.random.normal(jax.random.fold_in(_tk, 500 + 17), (12500, 128), jnp.float32)
        tbl_18 = 0.05 * jax.random.normal(jax.random.fold_in(_tk, 500 + 18), (1250, 128), jnp.float32)
        tbl_19 = 0.05 * jax.random.normal(jax.random.fold_in(_tk, 500 + 19), (12500, 128), jnp.float32)
        tbl_20 = 0.05 * jax.random.normal(jax.random.fold_in(_tk, 500 + 20), (12500, 128), jnp.float32)
        tbl_21 = 0.05 * jax.random.normal(jax.random.fold_in(_tk, 500 + 21), (1250, 128), jnp.float32)
        tbl_22 = 0.05 * jax.random.normal(jax.random.fold_in(_tk, 500 + 22), (1250, 128), jnp.float32)
        tbl_23 = 0.05 * jax.random.normal(jax.random.fold_in(_tk, 500 + 23), (1000, 128), jnp.float32)
        tbl_24 = 0.05 * jax.random.normal(jax.random.fold_in(_tk, 500 + 24), (1250, 128), jnp.float32)
        tbl_25 = 0.05 * jax.random.normal(jax.random.fold_in(_tk, 500 + 25), (1250, 128), jnp.float32)
        _rk = jax.random.fold_in(_tk, 7)
        r_dense = -0.000520686 + 1.00062 * jax.random.normal(jax.random.fold_in(_rk, 101), (512, 128), jnp.float32)
        W_top1 = 0.0456912 * jax.random.normal(jax.random.fold_in(_tk, 801), (479, 512), jnp.float32)
        W_top2 = 0.0441942 * jax.random.normal(jax.random.fold_in(_tk, 802), (512, 256), jnp.float32)
        W_top3 = 0.0625 * jax.random.normal(jax.random.fold_in(_tk, 803), (256, 1), jnp.float32)
        b_top1 = jnp.zeros((512,), jnp.float32)
        b_top2 = jnp.zeros((256,), jnp.float32)
        return (r_dense, ids, tbl_0, tbl_1, tbl_2, tbl_3, tbl_4, tbl_5, tbl_6, tbl_7, tbl_8, tbl_9, tbl_10, tbl_11, tbl_12, tbl_13, tbl_14, tbl_15, tbl_16, tbl_17, tbl_18, tbl_19, tbl_20, tbl_21, tbl_22, tbl_23, tbl_24, tbl_25, W_top1, b_top1, W_top2, b_top2, W_top3)
    r_dense, ids, tbl_0, tbl_1, tbl_2, tbl_3, tbl_4, tbl_5, tbl_6, tbl_7, tbl_8, tbl_9, tbl_10, tbl_11, tbl_12, tbl_13, tbl_14, tbl_15, tbl_16, tbl_17, tbl_18, tbl_19, tbl_20, tbl_21, tbl_22, tbl_23, tbl_24, tbl_25, W_top1, b_top1, W_top2, b_top2, W_top3 = _rec_inputs()

    def _L0_rec_setup():
        import jax, jax.numpy as jnp
        import numpy as np
        B, NUM_EMBS, D = (2048, 26, 128)
        key = jax.random.key(seed)
        k1, k2 = jax.random.split(key)
        dense = jax.random.normal(k1, (B, D), dtype=jnp.float32)
        embs = jax.random.normal(k2, (B, NUM_EMBS, D), dtype=jnp.float32)
        return {'dense': dense, 'embs': embs}
    _L0_rec_all = _L0_rec_setup()
    _L0_rec_in = {k: v for k, v in _L0_rec_all.items() if k in ()}
    del _L0_rec_all
    return {'r_dense': r_dense, 'ids': ids, 'tbl_0': tbl_0, 'tbl_1': tbl_1, 'tbl_2': tbl_2, 'tbl_3': tbl_3, 'tbl_4': tbl_4, 'tbl_5': tbl_5, 'tbl_6': tbl_6, 'tbl_7': tbl_7, 'tbl_8': tbl_8, 'tbl_9': tbl_9, 'tbl_10': tbl_10, 'tbl_11': tbl_11, 'tbl_12': tbl_12, 'tbl_13': tbl_13, 'tbl_14': tbl_14, 'tbl_15': tbl_15, 'tbl_16': tbl_16, 'tbl_17': tbl_17, 'tbl_18': tbl_18, 'tbl_19': tbl_19, 'tbl_20': tbl_20, 'tbl_21': tbl_21, 'tbl_22': tbl_22, 'tbl_23': tbl_23, 'tbl_24': tbl_24, 'tbl_25': tbl_25, 'W_top1': W_top1, 'b_top1': b_top1, 'W_top2': W_top2, 'b_top2': b_top2, 'W_top3': W_top3}

def reference(r_dense, ids, tbl_0, tbl_1, tbl_2, tbl_3, tbl_4, tbl_5, tbl_6, tbl_7, tbl_8, tbl_9, tbl_10, tbl_11, tbl_12, tbl_13, tbl_14, tbl_15, tbl_16, tbl_17, tbl_18, tbl_19, tbl_20, tbl_21, tbl_22, tbl_23, tbl_24, tbl_25, W_top1, b_top1, W_top2, b_top2, W_top3):
    import jax
    import jax.numpy as jnp

    def _L0_rec_ref(dense, embs):
        import jax, jax.numpy as jnp
        import numpy as np
        B, NUM_EMBS, D = (2048, 26, 128)
        T = jnp.concatenate([dense[:, None, :], embs], axis=1)
        N = T.shape[1]
        Z = jnp.einsum('bnd,bmd->bnm', T, T)
        iu0, iu1 = jnp.triu_indices(N, k=1)
        return Z[:, iu0, iu1]
    e = jnp.stack([tbl_0[ids[:, 0]], tbl_1[ids[:, 1]], tbl_2[ids[:, 2]], tbl_3[ids[:, 3]], tbl_4[ids[:, 4]], tbl_5[ids[:, 5]], tbl_6[ids[:, 6]], tbl_7[ids[:, 7]], tbl_8[ids[:, 8]], tbl_9[ids[:, 9]], tbl_10[ids[:, 10]], tbl_11[ids[:, 11]], tbl_12[ids[:, 12]], tbl_13[ids[:, 13]], tbl_14[ids[:, 14]], tbl_15[ids[:, 15]], tbl_16[ids[:, 16]], tbl_17[ids[:, 17]], tbl_18[ids[:, 18]], tbl_19[ids[:, 19]], tbl_20[ids[:, 20]], tbl_21[ids[:, 21]], tbl_22[ids[:, 22]], tbl_23[ids[:, 23]], tbl_24[ids[:, 24]], tbl_25[ids[:, 25]]], axis=1)
    z = _L0_rec_ref(r_dense, e)
    z = z.reshape(z.shape[0], -1)
    h = jnp.concatenate([z, r_dense], axis=1)
    h = jnp.maximum(h @ W_top1 + b_top1, 0.0)
    h = jnp.maximum(h @ W_top2 + b_top2, 0.0)
    y = h @ W_top3
    return y

_drawn_inputs = setup_inputs


def setup_inputs(seed=0):
    import zlib

    import numpy as np

    out = dict(_drawn_inputs(seed))
    spreads = {'b_top1': (0.0, 0.1), 'b_top2': (0.0, 0.1)}
    factors = {}
    for name, (base, spread) in spreads.items():
        noise = np.random.default_rng([zlib.crc32(name.encode()), seed]).standard_normal(out[name].shape)
        drawn = base * np.exp(spread * noise) if base else spread * noise
        out[name] = jnp.asarray(drawn.astype(out[name].dtype))
    for name, factor in factors.items():
        out[name] = (out[name] * factor).astype(out[name].dtype)
    return out
```

```python
from contextlib import ExitStack

import concourse.bass as bass
from concourse import mybir

P = 128
BATCH = 512
TILES = BATCH // P
D = 128
SIZES = [12500, 125000, 1250, 12500, 1000, 1000, 1000, 12500, 12500, 1250, 12500, 1250, 1000, 1250, 1250, 1250, 1000,
         12500, 1250, 12500, 12500, 1250, 1250, 1000, 1250, 1250]
FIELDS = len(SIZES)
PLACES = FIELDS + 1
PAD = 32
SAMPLES = 4
H1 = 512
H2 = 256

ONEHOT = [4, 5, 6, 12, 16, 23]
K_OH = len(ONEHOT)
OH_ROWS = 125
OH_CHUNKS = [SIZES[f] // OH_ROWS for f in ONEHOT]
KINDS = sorted(set(OH_CHUNKS))
MOST = max(OH_CHUNKS)
TABLES = 3
HEAD = 2
PARTS = 3
HOTS = 8
ACT_EVERY = 4
MERGED = 3

GATHERED = [f for f in range(FIELDS) if f not in ONEHOT]
PLACE_FIELDS = ONEHOT + GATHERED
FIRST = 1 + K_OH
ROW_TILES = 2
GROUPS = [(a, min(4, PLACES - a)) for a in range(FIRST, PLACES, 4)]

CHUNKS = 4
LOW = FIELDS - 4 * CHUNKS
SHARED = 3
LOW_AT = 4 * SHARED + LOW
LOW_DMAS = 4
BIAS_AT = P - 1
HALVES = 4
QH = P // SAMPLES // HALVES
ACT_SAMPLES = 2


WARM_UP = 24


def timeline():
    steps = [("dense", 0, 0)]
    for i in range(K_OH):
        steps.append(("onehot", 0, i))
        if i >= K_OH - MERGED:
            steps.append(("rows", 0, i - (K_OH - MERGED)))
    steps += [("rows", 0, g) for g in range(MERGED, len(GROUPS))]
    for t in range(1, TILES):
        steps += [("gram", t - 1, 0), ("gram", t - 1, 1), ("rows", t, 0), ("gram", t - 1, 2), ("gram", t - 1, 3)]
        if t >= 2:
            steps += [("turn", t - 2, 0), ("rows", t, 1), ("rows", t, 2), ("layer2", t - 2, 0)]
        else:
            steps += [("rows", t, 1), ("rows", t, 2)]
        steps += [("rows", t, 3), ("layer1", t - 1, 0)]
        steps += [("rows", t, g) for g in range(4, len(GROUPS))]
        steps += [("layer1", t - 1, 1)]
    t = TILES - 1
    steps += [("gram", t, 0), ("gram", t, 1), ("turn", t - 1, 0), ("gram", t, 2), ("gram", t, 3)]
    steps += [("layer2", t - 1, 0), ("layer1", t, 0), ("layer1", t, 1), ("turn", t, 0), ("layer2", t, 0)]
    return steps


STEPS = timeline()


def banks_filled(step):
    return sum(kind in ("dense", "onehot", "rows", "turn") for kind, _, _ in STEPS[:STEPS.index(step) + 1])


def transposes(step):
    return sum(kind in ("dense", "rows", "turn") for kind, _, _ in STEPS[:STEPS.index(step) + 1])


def first_hot(i):
    return sum(OH_CHUNKS[:i])


def split_parts(i, c):
    return 1 if i == 0 and c < HEAD else i + 2


def by_scalar(k):
    return k % ACT_EVERY == ACT_EVERY - 1


def hots_made(k, scalar):
    return sum(by_scalar(x) == scalar for x in range(k + 1))


def dlrm_tower(nc, dense, ids, ids_oh, tbls, w1, w2, b2, w3, out):
    f32, f32r, i32 = mybir.dt.float32, mybir.dt.float32r, mybir.dt.int32
    ALU, ACT = mybir.AluOpType, mybir.ActivationFunctionType
    with ExitStack() as ctx:
        def sb(name, shape, dt=f32):
            return ctx.enter_context(nc.sbuf_tensor(name, shape, dt))

        def pb(name, shape):
            return ctx.enter_context(nc.psum_tensor(name, shape, f32))

        def sem(name):
            return ctx.enter_context(nc.semaphore(name))

        idx = sb("idx", [P, TILES, FIELDS], i32)
        dense_sb = sb("dense_sb", [P, TILES, D])
        rows = sb("rows", [P, ROW_TILES, len(GATHERED), D])
        XT = sb("XT", [P, BATCH, PAD])
        Zt = sb("Zt", [P, CHUNKS, BATCH])
        Zlow = sb("Zlow", [LOW, 2, LOW, P])
        w1_sb = sb("w1_sb", [P, CHUNKS + 1, H1])
        w2_sb = sb("w2_sb", [P, H1 // P, H2])
        b2_sb = sb("b2_sb", [P, H2])
        w3_sb = sb("w3_sb", [P, H2])
        ident = sb("ident", [P, P])
        h1 = sb("h1", [P, H1])
        h1T = sb("h1T", [P, H1 // P, P])
        h2 = sb("h2", [P, H2])
        h2w = sb("h2w", [P, H2])
        y = sb("y", [P, TILES])
        ids_bc = sb("ids_bc", [OH_ROWS, TABLES, BATCH], i32)
        rownum_i = sb("rownum_i", [OH_ROWS, len(KINDS), MOST], i32)
        rownum = sb("rownum", [OH_ROWS, len(KINDS), MOST])
        minus_row = sb("minus_row", [OH_ROWS, len(KINDS), MOST])
        table = sb("table", [OH_ROWS, TABLES, MOST * D])
        t_hi = sb("t_hi", [OH_ROWS, PARTS, MOST * D], f32r)
        t_lo = sb("t_lo", [OH_ROWS, PARTS, MOST * D], f32r)
        hot = sb("hot", [OH_ROWS, HOTS, BATCH], f32r)
        apart = sb("apart", [OH_ROWS, 2, BATCH])
        tp = pb("tp", [P, 2, BATCH])
        gr = pb("gr", [P, 2, QH, SAMPLES, PAD])
        l1 = pb("l1", [P, H1])
        l2 = pb("l2", [P, 2 * H2])

        idx_in, dense_in, w1_in, w2_in = sem("idx_in"), sem("dense_in"), sem("w1_in"), sem("w2_in")
        ids_in = [sem(f"ids_in{i}") for i in range(K_OH)]
        table_in = [sem(f"table_in{i}") for i in range(K_OH)]
        rows_in = [[sem(f"rows_in{t}_{g}") for g in range(len(GROUPS))] for t in range(TILES)]
        low_in = [sem(f"low_in{t}") for t in range(TILES)]
        y_out = sem("y_out")
        ident_zero, ident_ready, xt_ready, zt_ready = (
            sem("ident_zero"), sem("ident_ready"), sem("xt_ready"), sem("zt_ready"))
        iota_ready, rownum_ready = sem("iota_ready"), sem("rownum_ready")
        hi_ready, lo_ready, apart_ready = sem("hi_ready"), sem("lo_ready"), sem("apart_ready")
        hot_dve, hot_act, hot_used = sem("hot_dve"), sem("hot_act"), sem("hot_used")
        tp_full, tp_empty = sem("tp_full"), sem("tp_empty")
        gram_full, gram_dve, gram_act = sem("gram_full"), sem("gram_dve"), sem("gram_act")
        l1_full, h1_ready, l2_full = sem("l1_full"), sem("h1_ready"), sem("l2_full")
        h2_sum, y_ready = sem("h2_sum"), sem("y_ready")

        block = ctx.enter_context(nc.Block())

        @block.sync
        def _(sp):
            sp.dma_start(idx[:], ids.rearrange("(t p) f -> p t f", p=P)).then_inc(idx_in, 16)
            for i, f in enumerate(ONEHOT):
                n = OH_CHUNKS[i]
                if i >= TABLES:
                    sp.wait_ge(lo_ready, split_parts(i - TABLES, MOST))
                sp.dma_start(table[:, i % TABLES, 0:n * D],
                             tbls[f].rearrange("(p c) d -> p (c d)", c=n)).then_inc(table_in[i], 16)
                if i >= TABLES:
                    sp.wait_ge(hot_used, first_hot(i - TABLES + 1))
                sp.dma_start(ids_bc[:, i % TABLES, :],
                             ids_oh[i:i + 1, :].broadcast_to((OH_ROWS, BATCH))).then_inc(ids_in[i], 16)
                if i == 0:
                    sp.dma_start(dense_sb[:], dense.rearrange("(t p) d -> p t d", p=P)).then_inc(dense_in, 16)
            sp.dma_start(w1_sb[:], w1).then_inc(w1_in, 16)
            sp.dma_start(w2_sb[:], w2.rearrange("(j p) k -> p j k", p=P)).then_inc(w2_in, 16)
            sp.dma_start(b2_sb[:], b2.rearrange("(o k) -> o k", o=1).broadcast_to((P, H2))).then_inc(w2_in, 16)
            sp.dma_start(w3_sb[:], w3.rearrange("k o -> o k").broadcast_to((P, H2))).then_inc(w2_in, 16)

            def low_stars(t):
                sp.wait_ge(gram_dve, HALVES * (t + 1))
                sp.wait_ge(gram_act, HALVES * (t + 1))
                tile = slice(t * P, (t + 1) * P)
                for g in range(LOW_DMAS):
                    sp.dma_start(Zt[32 * g + LOW_AT:32 * g + LOW_AT + LOW, 0:-(-(LOW - g) // 4), tile],
                                 Zlow[:, t % 2, g:LOW:4, :]).then_inc(low_in[t], 16)

            def result(t):
                sp.wait_ge(y_ready, t + 1)
                with nc.allow_non_contiguous_dma(reason="one value per sample"):
                    sp.dma_start(out[t * P:(t + 1) * P, :], y[:, t:t + 1]).then_inc(y_out, 16)

            for t in range(TILES):
                low_stars(t)
                if t:
                    result(t - 1)
            result(TILES - 1)
            sp.wait_ge(y_out, 16 * TILES)

        @block.gpsimd
        def _(pool):
            nc.gpsimd.memset(ident[:], 0.0).then_inc(ident_zero, 1)
            for v, n in enumerate(KINDS):
                nc.gpsimd.iota(rownum_i[:, v, :], pattern=[[1, MOST]], base=0,
                               channel_multiplier=n).then_inc(iota_ready, 1)
            pool.wait_ge(ident_zero, 1)
            nc.gpsimd.affine_select(out=ident[:], in_=ident[:], compare_op=ALU.not_equal, fill=1.0, base=0,
                                    pattern=[[-1, P]], channel_multiplier=1).then_inc(ident_ready, 1)
            pool.wait_ge(idx_in, 16)
            for t in range(TILES):
                for g, (a, n) in enumerate(GROUPS):
                    if t >= ROW_TILES:
                        pool.wait_ge(tp_full, transposes(("rows", t - ROW_TILES, g)))
                    for place in range(a, a + n):
                        f = PLACE_FIELDS[place - 1]
                        nc.gpsimd.indirect_dma_start(
                            rows[:, t % ROW_TILES, place - FIRST, :], None, tbls[f],
                            bass.IndirectOffsetOnAxis(ap=idx[:, t, f:f + 1], axis=0)).then_inc(rows_in[t][g], 16)

        @block.tensor
        def _(pe):
            banks, halves = 0, 0
            pe.wait_ge(ident_ready, 1)
            for _ in range(WARM_UP):
                nc.tensor.transpose(l2[:, 0:P], ident[:], ident[:])
            for kind, t, i in STEPS:
                tile = slice(t * P, (t + 1) * P)
                bank = banks % 2
                if kind in ("dense", "rows", "onehot", "turn"):
                    if banks >= 2:
                        pe.wait_ge(tp_empty, banks - 1)
                    banks += 1
                if kind == "dense":
                    pe.wait_ge(dense_in, 16)
                    for j in range(TILES):
                        last = nc.tensor.transpose(tp[:, bank, j * P:(j + 1) * P], dense_sb[:, j, :], ident[:])
                    last.then_inc(tp_full, 1)
                elif kind == "rows":
                    a, n = GROUPS[i]
                    pe.wait_ge(rows_in[t][i], 16 * n)
                    for j in range(n):
                        last = nc.tensor.transpose(tp[:, bank, j * P:(j + 1) * P],
                                                   rows[:, t % ROW_TILES, a + j - FIRST, :], ident[:])
                    last.then_inc(tp_full, 1)
                elif kind == "onehot":
                    n = OH_CHUNKS[i]
                    for c in range(n):
                        k = first_hot(i) + c
                        pe.wait_ge(hi_ready, split_parts(i, c))
                        pe.wait_ge(lo_ready, split_parts(i, c))
                        pe.wait_ge(hot_act if by_scalar(k) else hot_dve, hots_made(k, by_scalar(k)))
                        nc.tensor.matmul(tp[:, bank, :], t_hi[:, i % PARTS, c * D:(c + 1) * D], hot[:, k % HOTS, :],
                                         start=c == 0, stop=False)
                        nc.tensor.matmul(tp[:, bank, :], t_lo[:, i % PARTS, c * D:(c + 1) * D], hot[:, k % HOTS, :],
                                         start=False, stop=c == n - 1).then_inc(hot_used, 1)
                elif kind == "gram":
                    pe.wait_ge(tp_empty, banks_filled(("rows", t, len(GROUPS) - 1)))
                    if halves == 0:
                        pe.wait_ge(xt_ready, 1)
                    if halves >= 2:
                        pe.wait_ge(gram_dve, halves - 1)
                        pe.wait_ge(gram_act, halves - 1)
                    for q in range(QH):
                        b = t * P + SAMPLES * (i * QH + q)
                        last = nc.tensor.matmul(gr[:, halves % 2, q, :, 0:FIELDS],
                                                XT[:, b:b + SAMPLES, :].rearrange("d s n -> d (s n)"),
                                                XT[:, b:b + SAMPLES, 1:PLACES], start=True, stop=True)
                    last.then_inc(gram_full, 1)
                    halves += 1
                elif kind == "layer1" and i == 0:
                    if t == 0:
                        pe.wait_ge(w1_in, 16)
                    else:
                        pe.wait_ge(h1_ready, t)
                    nc.tensor.matmul(l1[:], XT[:, tile, 0], w1_sb[:, CHUNKS, :], start=True, stop=False)
                    pe.wait_ge(gram_dve, halves)
                    pe.wait_ge(gram_act, halves)
                    for c in range(SHARED, CHUNKS):
                        nc.tensor.matmul(l1[:], Zt[:, c, tile], w1_sb[:, c, :], start=False, stop=False)
                elif kind == "layer1":
                    pe.wait_ge(low_in[t], 16 * LOW_DMAS)
                    for c in range(SHARED):
                        last = nc.tensor.matmul(l1[:], Zt[:, c, tile], w1_sb[:, c, :], start=False,
                                                stop=c == SHARED - 1)
                    last.then_inc(l1_full, 1)
                elif kind == "turn":
                    pe.wait_ge(h1_ready, t + 1)
                    for j in range(H1 // P):
                        last = nc.tensor.transpose(tp[:, bank, j * P:(j + 1) * P], h1[:, j * P:(j + 1) * P],
                                                   ident[:])
                    last.then_inc(tp_full, 1)
                elif kind == "layer2":
                    if t == 0:
                        pe.wait_ge(w2_in, 3 * 16)
                    else:
                        pe.wait_ge(h2_sum, t)
                    pe.wait_ge(tp_empty, banks_filled(("turn", t, 0)))
                    for j in range(H1 // P):
                        last = nc.tensor.matmul(l2[:, 0:H2], h1T[:, j, :], w2_sb[:, j, :], start=j == 0,
                                                stop=j == H1 // P - 1)
                    last.then_inc(l2_full, 1)

        def copy_gram(copy, t, h, half, samples):
            for s in samples:
                first = h * QH * SAMPLES + s
                end = first + (QH - 1) * SAMPLES + 1
                for g in range(4):
                    copy(Zt[32 * g:32 * g + PLACES, :, t * P + first:t * P + end:SAMPLES].rearrange("n c q -> n q c"),
                         gr[32 * s:32 * s + PLACES, half, :, s, LOW + g:FIELDS:4])
                last = copy(Zlow[:, t % 2, :, first:end:SAMPLES].rearrange("n m q -> n q m"),
                            gr[32 * s:32 * s + LOW, half, :, s, 0:LOW])
            return last

        @block.scalar
        def _(act):
            banks, halves = 0, 0

            def high_part(i, c0, c1):
                act.wait_ge(table_in[i], 16)
                if i >= PARTS:
                    act.wait_ge(hot_used, first_hot(i - PARTS + 1))
                nc.scalar.copy(t_hi[:, i % PARTS, c0 * D:c1 * D],
                               table[:, i % TABLES, c0 * D:c1 * D]).then_inc(hi_ready, 1)

            def one_hot(i, k):
                made, c = hots_made(k, True), k - first_hot(i)
                act.wait_ge(ids_in[i], 16)
                act.wait_ge(rownum_ready, 2)
                if made > 2:
                    act.wait_ge(hot_act, made - 2)
                nc.scalar.activation(apart[:, made % 2, :], ids_bc[:, i % TABLES, :], ACT.Abs,
                                     bias=minus_row[:, KINDS.index(OH_CHUNKS[i]), c:c + 1]).then_inc(apart_ready, 1)
                act.wait_ge(apart_ready, made)
                if k >= HOTS:
                    act.wait_ge(hot_used, k - HOTS + 1)
                nc.scalar.activation(hot[:, k % HOTS, :], apart[:, made % 2, :], ACT.Relu, bias=1.0,
                                     scale=-1.0).then_inc(hot_act, 1)

            mine = [[k for k in range(first_hot(i), first_hot(i + 1)) if by_scalar(k)] for i in range(K_OH)]
            high_part(0, 0, HEAD)
            high_part(0, HEAD, OH_CHUNKS[0])
            one_hot(0, mine[0][0])
            high_part(1, 0, OH_CHUNKS[1])
            for kind, t, i in STEPS:
                if kind == "onehot":
                    for k in mine[i][1:]:
                        one_hot(i, k)
                    if i + 2 < K_OH:
                        high_part(i + 2, 0, OH_CHUNKS[i + 2])
                    if i + 1 < K_OH:
                        one_hot(i + 1, mine[i + 1][0])
                    act.wait_ge(hot_used, first_hot(i + 1))
                    nc.scalar.copy(XT[:, :, 1 + i], tp[:, banks % 2, :]).then_inc(tp_empty, 1)
                    banks += 1
                elif kind == "gram":
                    if halves == 0:
                        act.wait_ge(zt_ready, 1)
                    if i == 0 and t >= 2:
                        act.wait_ge(low_in[t - 2], 16 * LOW_DMAS)
                    act.wait_ge(gram_full, halves + 1)
                    copy_gram(nc.scalar.copy, t, i, halves % 2,
                              range(SAMPLES - ACT_SAMPLES, SAMPLES)).then_inc(gram_act, 1)
                    halves += 1
                elif kind in ("dense", "rows", "turn"):
                    act.wait_ge(tp_full, transposes((kind, t, i)))
                    if kind == "dense":
                        nc.scalar.copy(XT[:, :, 0], tp[:, banks % 2, :]).then_inc(tp_empty, 1)
                    elif kind == "rows":
                        a, n = GROUPS[i]
                        nc.scalar.copy(
                            XT[:, t * P:(t + 1) * P, a:a + n],
                            tp[:, banks % 2, 0:n * P].rearrange("p (n b) -> p b n", n=n)).then_inc(tp_empty, 1)
                    else:
                        nc.scalar.copy(h1T[:].rearrange("p j b -> p (j b)"), tp[:, banks % 2, :]).then_inc(tp_empty, 1)
                    banks += 1

        @block.vector
        def _(dve):
            halves = 0
            nc.vector.memset(Zt[:], 1.0).then_inc(zt_ready, 1)
            dve.wait_ge(iota_ready, len(KINDS))
            nc.vector.tensor_copy(rownum[:], rownum_i[:]).then_inc(rownum_ready, 1)
            nc.vector.tensor_scalar(minus_row[:], rownum_i[:], -1.0, None, ALU.mult).then_inc(rownum_ready, 1)
            dve.wait_ge(rownum_ready, 2)

            def low_part(i, c0, c1):
                dve.wait_ge(hi_ready, split_parts(i, c0))
                if i >= PARTS:
                    dve.wait_ge(hot_used, first_hot(i - PARTS + 1))
                nc.vector.tensor_tensor(t_lo[:, i % PARTS, c0 * D:c1 * D], table[:, i % TABLES, c0 * D:c1 * D],
                                        t_hi[:, i % PARTS, c0 * D:c1 * D].bitcast(f32),
                                        ALU.subtract).then_inc(lo_ready, 1)

            for kind, t, i in STEPS:
                if kind == "onehot":
                    dve.wait_ge(ids_in[i], 16)
                    for c in range(OH_CHUNKS[i]):
                        if i == 0 and c in (1, HEAD + 1):
                            low_part(0, *((0, HEAD) if c == 1 else (HEAD, OH_CHUNKS[0])))
                        if i + 1 < K_OH and c == OH_CHUNKS[i] // 2 + 1:
                            low_part(i + 1, 0, OH_CHUNKS[i + 1])
                        k = first_hot(i) + c
                        if not by_scalar(k):
                            if k >= HOTS:
                                dve.wait_ge(hot_used, k - HOTS + 1)
                            nc.vector.tensor_scalar(hot[:, k % HOTS, :], ids_bc[:, i % TABLES, :],
                                                    rownum[:, KINDS.index(OH_CHUNKS[i]), c:c + 1], None,
                                                    ALU.is_equal).then_inc(hot_dve, 1)
                    if i == K_OH - 1:
                        nc.vector.memset(XT[:, :, PLACES:PAD], 0.0).then_inc(xt_ready, 1)
                elif kind == "gram":
                    if halves == 0:
                        dve.wait_ge(zt_ready, 1)
                    if i == 0 and t >= 2:
                        dve.wait_ge(low_in[t - 2], 16 * LOW_DMAS)
                    dve.wait_ge(gram_full, halves + 1)
                    copy_gram(nc.vector.tensor_copy, t, i, halves % 2,
                              range(SAMPLES - ACT_SAMPLES)).then_inc(gram_dve, 1)
                    halves += 1
                elif kind == "layer1" and i == 1:
                    dve.wait_ge(l1_full, t + 1)
                    if t:
                        dve.wait_ge(l2_full, t)
                    nc.vector.tensor_scalar(h1[:], l1[:], 0.0, None, ALU.max).then_inc(h1_ready, 1)
                elif kind == "layer2":
                    dve.wait_ge(l2_full, t + 1)
                    if t == 0:
                        dve.wait_ge(w2_in, 3 * 16)
                    else:
                        dve.wait_ge(y_ready, t)
                    nc.vector.tensor_tensor(h2[:], l2[:, 0:H2], b2_sb[:], ALU.add).then_inc(h2_sum, 1)
                    dve.wait_ge(h2_sum, t + 1)
                    nc.vector.scalar_tensor_tensor(out=h2w[:], in0=h2[:], scalar=0.0, in1=w3_sb[:], op0=ALU.max,
                                                   op1=ALU.mult, accum_out=y[:, t:t + 1]).then_inc(y_ready, 1)


def kernel(**inputs):
    import numpy as np
    import concourse.bacc as bacc
    from concourse import mybir as mb
    from concourse.bass_utils import run_bass_kernel_spmd as run

    nc = bacc.Bacc("TRN2", target_bir_lowering=False, num_devices=1)
    place_of = {0: 0, **{f + 1: 1 + i for i, f in enumerate(PLACE_FIELDS)}}
    top1 = np.asarray(inputs["W_top1"])
    w1 = np.zeros((P, CHUNKS + 1, H1), top1.dtype)
    pairs = [sorted((place_of[n], place_of[m])) for n in range(PLACES) for m in range(n + 1, PLACES)]
    for row, (n, m) in enumerate(pairs):
        if m > LOW:
            c, g = divmod(m - LOW - 1, 4)
            w1[32 * g + n, c] = top1[row]
        else:
            c, g = divmod(m - 1, 4)
            w1[32 * g + LOW_AT + n, c] = top1[row]
    w1[BIAS_AT, CHUNKS - 1] = np.asarray(inputs["b_top1"])
    w1[:, CHUNKS] = top1[len(pairs):]
    ids = np.asarray(inputs["ids"])
    arrays = {"dense": inputs["r_dense"], "ids": ids, "ids_oh": ids[:, ONEHOT].T, "w1": w1, "w2": inputs["W_top2"],
              "b2": inputs["b_top2"], "w3": inputs["W_top3"]}
    arrays.update({f"tbl_{f}": inputs[f"tbl_{f}"] for f in range(FIELDS)})
    arrays = {n: np.ascontiguousarray(a) for n, a in arrays.items()}
    aps = {n: nc.dram_tensor(n, a.shape, mb.dt.from_np(a.dtype), kind="ExternalInput").ap() for n, a in arrays.items()}
    out = nc.dram_tensor("y_out_dram", (BATCH, 1), mb.dt.float32, kind="ExternalOutput").ap()
    dlrm_tower(nc, aps["dense"], aps["ids"], aps["ids_oh"], [aps[f"tbl_{f}"] for f in range(FIELDS)], aps["w1"],
               aps["w2"], aps["b2"], aps["w3"], out)
    r = run(nc, [arrays], core_ids=[0])
    return r.results[0]["y_out_dram"]
```

```python
from contextlib import ExitStack

import concourse.bass as bass
from concourse import mybir

P = 128
BATCH = 512
TILES = BATCH // P
D = 128
SIZES = [12500, 125000, 1250, 12500, 1000, 1000, 1000, 12500, 12500, 1250, 12500, 1250, 1000, 1250, 1250, 1250, 1000,
         12500, 1250, 12500, 12500, 1250, 1250, 1000, 1250, 1250]
FIELDS = len(SIZES)
PLACES = FIELDS + 1
PAD = 32
SAMPLES = 4
H1 = 512
H2 = 256

ONEHOT = [4, 5, 6, 12, 16, 23, 2, 9]
K_OH = len(ONEHOT)
OH_ROWS = 125
OH_CHUNKS = [SIZES[f] // OH_ROWS for f in ONEHOT]
KINDS = sorted(set(OH_CHUNKS))
MOST = max(OH_CHUNKS)
TABLES = 3
HEAD = 2
PARTS = 3
HOTS = 8
ACT_EVERY = 4
ROWS_AFTER = {K_OH - 3: [0, 1], K_OH - 2: [2, 3, 4]}

GATHERED = [f for f in range(FIELDS) if f not in ONEHOT]
PLACE_FIELDS = ONEHOT + GATHERED
FIRST = 1 + K_OH
ROW_TILES = 2
GROUPS = [(a, min(4, PLACES - a)) for a in range(FIRST, PLACES, 4)]

CHUNKS = 3
QUADS = P // PAD
LOW = FIELDS - QUADS * CHUNKS
SMALL = LOW - QUADS * CHUNKS
HIGH_ROWS = [LOW + CHUNKS * (g + 1) for g in range(QUADS)]
LOW_ROWS = [LOW - CHUNKS * g for g in range(QUADS)]
LOW_AT = [PAD - n for n in LOW_ROWS]
SMALL_AT = LOW_AT[0] - SMALL
MOVES = QUADS + 1
BLOCKS = H1 // P
BIAS_AT = PAD + HIGH_ROWS[1]
HALVES = 4
QH = P // SAMPLES // HALVES
ACT_SAMPLES = 2


WARM_UP = 24


def timeline():
    steps = [("dense", 0, 0)]
    for i in range(K_OH):
        steps.append(("onehot", 0, i))
        steps += [("rows", 0, g) for g in ROWS_AFTER.get(i, [])]
    steps += [("rows", 1, 0), ("rows", 1, 1), ("gram", 0, 0), ("gram", 0, 1), ("rows", 1, 2), ("gram", 0, 2),
              ("rows", 1, 3), ("rows", 1, 4), ("gram", 0, 3)]
    steps += [("rows", 2, 0), ("gram", 1, 0), ("rows", 2, 1), ("gram", 1, 1), ("rows", 2, 2), ("gram", 1, 2),
              ("layer1", 0, 0), ("layer1", 0, 1), ("rows", 2, 3), ("gram", 1, 3), ("rows", 2, 4), ("layer2", 0, 0)]
    steps += [("gram", 2, 0), ("gram", 2, 1), ("rows", 3, 0), ("gram", 2, 2), ("gram", 2, 3), ("layer1", 1, 0),
              ("layer1", 1, 1), ("rows", 3, 1), ("rows", 3, 2), ("layer2", 1, 0), ("rows", 3, 3), ("rows", 3, 4)]
    steps += [("gram", 3, h) for h in range(HALVES)]
    steps += [("layer1", 2, 0), ("layer1", 2, 1), ("layer1", 3, 0), ("layer2", 2, 0), ("layer1", 3, 1), ("layer2", 3, 0)]
    return steps


STEPS = timeline()


def banks_filled(step):
    return sum(kind in ("dense", "rows") for kind, _, _ in STEPS[:STEPS.index(step) + 1])


def first_hot(i):
    return sum(OH_CHUNKS[:i])


def split_parts(i, c):
    return 1 if i == 0 and c < HEAD else i + 2


def units_ready(t, u):
    return t + 1 + (u if t == TILES - 1 else 0)


def by_scalar(k):
    return k % ACT_EVERY == ACT_EVERY - 1


def hots_made(k, scalar):
    return sum(by_scalar(x) == scalar for x in range(k + 1))


def dlrm_tower(nc, dense, ids, ids_oh, tbls, w1, w2, b2, w3, out):
    f32, f32r, i32 = mybir.dt.float32, mybir.dt.float32r, mybir.dt.int32
    ALU, ACT = mybir.AluOpType, mybir.ActivationFunctionType
    with ExitStack() as ctx:
        def sb(name, shape, dt=f32):
            return ctx.enter_context(nc.sbuf_tensor(name, shape, dt))

        def pb(name, shape):
            return ctx.enter_context(nc.psum_tensor(name, shape, f32))

        def sem(name):
            return ctx.enter_context(nc.semaphore(name))

        idx = sb("idx", [P, TILES, FIELDS], i32)
        dense_sb = sb("dense_sb", [P, TILES, D])
        rows = sb("rows", [P, ROW_TILES, len(GATHERED), D])
        XT = sb("XT", [P, BATCH, PAD])
        Zt = sb("Zt", [P, CHUNKS, BATCH])
        Zlow = sb("Zlow", [LOW, 2, LOW, P])
        w1_sb = sb("w1_sb", [P, CHUNKS + 1, H1])
        w2_sb = sb("w2_sb", [P, BLOCKS, H2])
        b2_sb = sb("b2_sb", [P, H2])
        w3_sb = sb("w3_sb", [P, H2])
        ident = sb("ident", [P, P])
        h1 = sb("h1", [P, BLOCKS, P])
        h2 = sb("h2", [P, H2])
        h2w = sb("h2w", [P, H2])
        y = sb("y", [P, TILES])
        ids_bc = sb("ids_bc", [OH_ROWS, TABLES, BATCH], i32)
        rownum_i = sb("rownum_i", [OH_ROWS, len(KINDS), MOST], i32)
        rownum = sb("rownum", [OH_ROWS, len(KINDS), MOST])
        minus_row = sb("minus_row", [OH_ROWS, len(KINDS), MOST])
        table = sb("table", [OH_ROWS, TABLES, MOST * D])
        t_hi = sb("t_hi", [OH_ROWS, PARTS, MOST * D], f32r)
        t_lo = sb("t_lo", [OH_ROWS, PARTS, MOST * D], f32r)
        hot = sb("hot", [OH_ROWS, HOTS, BATCH], f32r)
        apart = sb("apart", [OH_ROWS, 2, BATCH])
        tp = pb("tp", [P, 2, BATCH])
        gr = pb("gr", [P, 2, QH, SAMPLES, PAD])
        l1 = pb("l1", [P, BLOCKS, P])
        l2 = pb("l2", [P, 2 * H2])

        idx_in, dense_in, w1_in, w2_in = sem("idx_in"), sem("dense_in"), sem("w1_in"), sem("w2_in")
        ids_in = [sem(f"ids_in{i}") for i in range(K_OH)]
        table_in = [sem(f"table_in{i}") for i in range(K_OH)]
        rows_in = [[sem(f"rows_in{t}_{g}") for g in range(len(GROUPS))] for t in range(TILES)]
        low_in = [sem(f"low_in{t}") for t in range(TILES)]
        y_out = sem("y_out")
        ident_zero, ident_ready, xt_ready, zt_ready = (
            sem("ident_zero"), sem("ident_ready"), sem("xt_ready"), sem("zt_ready"))
        iota_ready, rownum_ready = sem("iota_ready"), sem("rownum_ready")
        hi_ready, lo_ready, apart_ready = sem("hi_ready"), sem("lo_ready"), sem("apart_ready")
        hot_dve, hot_act, hot_used = sem("hot_dve"), sem("hot_act"), sem("hot_used")
        lookup_copied, tp_full, tp_empty = sem("lookup_copied"), sem("tp_full"), sem("tp_empty")
        gram_full, gram_dve, gram_act = sem("gram_full"), sem("gram_dve"), sem("gram_act")
        l1_full, h1_ready, l2_full = sem("l1_full"), sem("h1_ready"), sem("l2_full")
        h2_sum, y_ready = sem("h2_sum"), sem("y_ready")

        def lookup_bank(i):
            return l2[:] if i % 2 else l1[:].rearrange("p u b -> p (u b)")

        def l1_block(t, u):
            if t < TILES - 1:
                return l1[:, u, :]
            return gr[:].rearrange("p h q s n -> p (h q s n)")[:, u * 2 * H2:u * 2 * H2 + P]

        block = ctx.enter_context(nc.Block())


        @block.sync
        def _(sp):
            sp.dma_start(idx[:], ids.rearrange("(t p) f -> p t f", p=P)).then_inc(idx_in, 16)
            for i, f in enumerate(ONEHOT):
                n = OH_CHUNKS[i]
                if i >= TABLES:
                    sp.wait_ge(lo_ready, split_parts(i - TABLES, MOST))
                sp.dma_start(table[:, i % TABLES, 0:n * D],
                             tbls[f].rearrange("(p c) d -> p (c d)", c=n)).then_inc(table_in[i], 16)
                if i >= TABLES:
                    sp.wait_ge(hot_used, first_hot(i - TABLES + 1))
                sp.dma_start(ids_bc[:, i % TABLES, :],
                             ids_oh[i:i + 1, :].broadcast_to((OH_ROWS, BATCH))).then_inc(ids_in[i], 16)
                if i == 0:
                    sp.dma_start(dense_sb[:], dense.rearrange("(t p) d -> p t d", p=P)).then_inc(dense_in, 16)
            sp.dma_start(w1_sb[:], w1).then_inc(w1_in, 16)
            sp.dma_start(w2_sb[:], w2.rearrange("(j p) k -> p j k", p=P)).then_inc(w2_in, 16)
            sp.dma_start(b2_sb[:], b2.rearrange("(o k) -> o k", o=1).broadcast_to((P, H2))).then_inc(w2_in, 16)
            sp.dma_start(w3_sb[:], w3.rearrange("k o -> o k").broadcast_to((P, H2))).then_inc(w2_in, 16)


            def result(t):
                sp.wait_ge(y_ready, t + 1)
                with nc.allow_non_contiguous_dma(reason="one value per sample"):
                    sp.dma_start(out[t * P:(t + 1) * P, :], y[:, t:t + 1]).then_inc(y_out, 16)

            for t in range(TILES):
                sp.wait_ge(gram_dve, HALVES * (t + 1))
                sp.wait_ge(gram_act, HALVES * (t + 1))
                tile = slice(t * P, (t + 1) * P)
                for g in range(QUADS):
                    n = LOW_ROWS[g]
                    sp.dma_start(Zt[PAD * g + LOW_AT[g]:PAD * (g + 1), :, tile],
                                 Zlow[0:n, t % 2, n - CHUNKS:n, :]).then_inc(low_in[t], 16)
                sp.dma_start(Zt[SMALL_AT:SMALL_AT + SMALL, 0:SMALL, tile],
                             Zlow[0:SMALL, t % 2, 0:SMALL, :]).then_inc(low_in[t], 16)
                if t:
                    result(t - 1)
            result(TILES - 1)
            sp.wait_ge(y_out, 16 * TILES)

        @block.gpsimd
        def _(pool):
            nc.gpsimd.memset(ident[:], 0.0).then_inc(ident_zero, 1)
            for v, n in enumerate(KINDS):
                nc.gpsimd.iota(rownum_i[:, v, :], pattern=[[1, MOST]], base=0,
                               channel_multiplier=n).then_inc(iota_ready, 1)
            pool.wait_ge(ident_zero, 1)
            nc.gpsimd.affine_select(out=ident[:], in_=ident[:], compare_op=ALU.not_equal, fill=1.0, base=0,
                                    pattern=[[-1, P]], channel_multiplier=1).then_inc(ident_ready, 1)
            pool.wait_ge(idx_in, 16)
            for t in range(TILES):
                for g, (a, n) in enumerate(GROUPS):
                    if t >= ROW_TILES:
                        pool.wait_ge(tp_full, banks_filled(("rows", t - ROW_TILES, g)))
                    for place in range(a, a + n):
                        f = PLACE_FIELDS[place - 1]
                        nc.gpsimd.indirect_dma_start(
                            rows[:, t % ROW_TILES, place - FIRST, :], None, tbls[f],
                            bass.IndirectOffsetOnAxis(ap=idx[:, t, f:f + 1], axis=0)).then_inc(rows_in[t][g], 16)

        @block.tensor
        def _(pe):
            banks, halves = 0, 0

            def early_part(t, u):
                units, tile = slice(u * P, (u + 1) * P), slice(t * P, (t + 1) * P)
                nc.tensor.matmul(l1_block(t, u), w1_sb[:, CHUNKS, units], XT[:, tile, 0], start=True, stop=False)

            pe.wait_ge(ident_ready, 1)
            for _ in range(WARM_UP):
                nc.tensor.transpose(l2[:, 0:P], ident[:], ident[:])
            for kind, t, i in STEPS:
                tile = slice(t * P, (t + 1) * P)
                bank = banks % 2
                if kind in ("dense", "rows"):
                    if banks >= 2:
                        pe.wait_ge(tp_empty, banks - 1)
                    banks += 1
                if kind == "dense":
                    pe.wait_ge(dense_in, 16)
                    for j in range(TILES):
                        last = nc.tensor.transpose(tp[:, bank, j * P:(j + 1) * P], dense_sb[:, j, :], ident[:])
                    last.then_inc(tp_full, 1)
                elif kind == "rows":
                    a, n = GROUPS[i]
                    pe.wait_ge(rows_in[t][i], 16 * n)
                    for j in range(n):
                        last = nc.tensor.transpose(tp[:, bank, j * P:(j + 1) * P],
                                                   rows[:, t % ROW_TILES, a + j - FIRST, :], ident[:])
                    last.then_inc(tp_full, 1)
                elif kind == "onehot":
                    n = OH_CHUNKS[i]
                    if i >= 2:
                        pe.wait_ge(lookup_copied, i - 1)
                    for c in range(n):
                        k = first_hot(i) + c
                        pe.wait_ge(hi_ready, split_parts(i, c))
                        pe.wait_ge(lo_ready, split_parts(i, c))
                        pe.wait_ge(hot_act if by_scalar(k) else hot_dve, hots_made(k, by_scalar(k)))
                        nc.tensor.matmul(lookup_bank(i), t_hi[:, i % PARTS, c * D:(c + 1) * D], hot[:, k % HOTS, :],
                                         start=c == 0, stop=False)
                        nc.tensor.matmul(lookup_bank(i), t_lo[:, i % PARTS, c * D:(c + 1) * D], hot[:, k % HOTS, :],
                                         start=False, stop=c == n - 1).then_inc(hot_used, 1)
                elif kind == "gram":
                    pe.wait_ge(tp_empty, banks_filled(("rows", t, len(GROUPS) - 1)))
                    if halves == 0:
                        pe.wait_ge(lookup_copied, K_OH)
                        pe.wait_ge(xt_ready, 1)
                    if halves >= 2:
                        pe.wait_ge(gram_dve, halves - 1)
                        pe.wait_ge(gram_act, halves - 1)
                    for q in range(QH):
                        b = t * P + SAMPLES * (i * QH + q)
                        last = nc.tensor.matmul(gr[:, halves % 2, q, :, 0:FIELDS],
                                                XT[:, b:b + SAMPLES, :].rearrange("d s n -> d (s n)"),
                                                XT[:, b:b + SAMPLES, 1:PLACES], start=True, stop=True)
                    last.then_inc(gram_full, 1)
                    halves += 1
                elif kind == "layer1" and i == 0:
                    if t == 0:
                        pe.wait_ge(w1_in, 16)
                    elif t < TILES - 1:
                        pe.wait_ge(h1_ready, t)
                    pe.wait_ge(gram_dve, HALVES * (t + 1))
                    pe.wait_ge(gram_act, HALVES * (t + 1))
                    if t == TILES - 1:
                        for u in range(BLOCKS):
                            early_part(t, u)
                elif kind == "layer1":
                    pe.wait_ge(low_in[t], 16 * MOVES)
                    for u in range(BLOCKS):
                        if t < TILES - 1:
                            early_part(t, u)
                        for c in range(CHUNKS):
                            last = nc.tensor.matmul(l1_block(t, u), w1_sb[:, c, u * P:(u + 1) * P], Zt[:, c, tile],
                                                    start=False, stop=c == CHUNKS - 1)
                        if t == TILES - 1 or u == BLOCKS - 1:
                            last.then_inc(l1_full, 1)
                elif kind == "layer2":
                    if t == 0:
                        pe.wait_ge(w2_in, 3 * 16)
                    else:
                        pe.wait_ge(h2_sum, t)
                    for u in range(BLOCKS):
                        pe.wait_ge(h1_ready, units_ready(t, u))
                        last = nc.tensor.matmul(l2[:, 0:H2], h1[:, u, :], w2_sb[:, u, :], start=u == 0,
                                                stop=u == BLOCKS - 1)
                    last.then_inc(l2_full, 1)

        def copy_gram(copy, t, h, half, samples):
            for s in samples:
                first = h * QH * SAMPLES + s
                end = first + (QH - 1) * SAMPLES + 1
                for g, n in enumerate(HIGH_ROWS):
                    copy(Zt[PAD * g:PAD * g + n, :, t * P + first:t * P + end:SAMPLES].rearrange("n c q -> n q c"),
                         gr[PAD * s:PAD * s + n, half, :, s, n - CHUNKS:n])
                last = copy(Zlow[:, t % 2, :, first:end:SAMPLES].rearrange("n m q -> n q m"),
                            gr[PAD * s:PAD * s + LOW, half, :, s, 0:LOW])
            return last

        @block.scalar
        def _(act):
            banks, halves = 0, 0

            def high_part(i, c0, c1):
                act.wait_ge(table_in[i], 16)
                if i >= PARTS:
                    act.wait_ge(hot_used, first_hot(i - PARTS + 1))
                nc.scalar.copy(t_hi[:, i % PARTS, c0 * D:c1 * D],
                               table[:, i % TABLES, c0 * D:c1 * D]).then_inc(hi_ready, 1)

            mine = [k for k in range(first_hot(K_OH)) if by_scalar(k)]
            table_of = [i for i in range(K_OH) for _ in range(OH_CHUNKS[i])]

            def distance(j):
                i = table_of[mine[j]]
                act.wait_ge(ids_in[i], 16)
                act.wait_ge(rownum_ready, 2)
                if j >= 2:
                    act.wait_ge(hot_act, j - 1)
                c = mine[j] - first_hot(i)
                nc.scalar.activation(apart[:, j % 2, :], ids_bc[:, i % TABLES, :], ACT.Abs,
                                     bias=minus_row[:, KINDS.index(OH_CHUNKS[i]), c:c + 1]).then_inc(apart_ready, 1)

            def one_hot(k):
                j = mine.index(k)
                act.wait_ge(apart_ready, j + 1)
                if k >= HOTS:
                    act.wait_ge(hot_used, k - HOTS + 1)
                nc.scalar.activation(hot[:, k % HOTS, :], apart[:, j % 2, :], ACT.Relu, bias=1.0,
                                     scale=-1.0).then_inc(hot_act, 1)
                if 0 < j < len(mine) - 1:
                    distance(j + 1)

            def mine_in(i):
                return [k for k in mine if table_of[k] == i]

            high_part(0, 0, HEAD)
            distance(0)
            high_part(0, HEAD, OH_CHUNKS[0])
            one_hot(mine_in(0)[0])
            high_part(1, 0, OH_CHUNKS[1])
            distance(1)
            for kind, t, i in STEPS:
                if kind == "onehot":
                    for k in mine_in(i)[1:]:
                        one_hot(k)
                    if i + 2 < K_OH:
                        high_part(i + 2, 0, OH_CHUNKS[i + 2])
                    if i + 1 < K_OH:
                        one_hot(mine_in(i + 1)[0])
                    act.wait_ge(hot_used, first_hot(i + 1))
                    nc.scalar.copy(XT[:, :, 1 + i], lookup_bank(i)).then_inc(lookup_copied, 1)
                elif kind == "gram":
                    if halves == 0:
                        act.wait_ge(zt_ready, 1)
                    if i == 0 and t >= 2:
                        act.wait_ge(low_in[t - 2], 16 * MOVES)
                    act.wait_ge(gram_full, halves + 1)
                    copy_gram(nc.scalar.copy, t, i, halves % 2,
                              range(SAMPLES - ACT_SAMPLES, SAMPLES)).then_inc(gram_act, 1)
                    halves += 1
                elif kind in ("dense", "rows"):
                    act.wait_ge(tp_full, banks_filled((kind, t, i)))
                    if kind == "dense":
                        nc.scalar.copy(XT[:, :, 0], tp[:, banks % 2, :]).then_inc(tp_empty, 1)
                    else:
                        a, n = GROUPS[i]
                        nc.scalar.copy(
                            XT[:, t * P:(t + 1) * P, a:a + n],
                            tp[:, banks % 2, 0:n * P].rearrange("p (n b) -> p b n", n=n)).then_inc(tp_empty, 1)
                    banks += 1

        @block.vector
        def _(dve):
            halves = 0
            nc.vector.memset(Zt[:], 1.0).then_inc(zt_ready, 1)
            dve.wait_ge(iota_ready, len(KINDS))
            nc.vector.tensor_copy(rownum[:], rownum_i[:]).then_inc(rownum_ready, 1)
            nc.vector.tensor_scalar(minus_row[:], rownum_i[:], -1.0, None, ALU.mult).then_inc(rownum_ready, 1)
            dve.wait_ge(rownum_ready, 2)

            def low_part(i, c0, c1):
                dve.wait_ge(hi_ready, split_parts(i, c0))
                if i >= PARTS:
                    dve.wait_ge(hot_used, first_hot(i - PARTS + 1))
                nc.vector.tensor_tensor(t_lo[:, i % PARTS, c0 * D:c1 * D], table[:, i % TABLES, c0 * D:c1 * D],
                                        t_hi[:, i % PARTS, c0 * D:c1 * D].bitcast(f32),
                                        ALU.subtract).then_inc(lo_ready, 1)

            for kind, t, i in STEPS:
                if kind == "onehot":
                    dve.wait_ge(ids_in[i], 16)
                    for c in range(OH_CHUNKS[i]):
                        if i == 0 and c in (1, HEAD + 1):
                            low_part(0, *((0, HEAD) if c == 1 else (HEAD, OH_CHUNKS[0])))
                        if i + 1 < K_OH and c == OH_CHUNKS[i] // 2 + 1:
                            low_part(i + 1, 0, OH_CHUNKS[i + 1])
                        k = first_hot(i) + c
                        if not by_scalar(k):
                            if k >= HOTS:
                                dve.wait_ge(hot_used, k - HOTS + 1)
                            nc.vector.tensor_scalar(hot[:, k % HOTS, :], ids_bc[:, i % TABLES, :],
                                                    rownum[:, KINDS.index(OH_CHUNKS[i]), c:c + 1], None,
                                                    ALU.is_equal).then_inc(hot_dve, 1)
                    if i == K_OH - 1:
                        nc.vector.memset(XT[:, :, PLACES:PAD], 0.0).then_inc(xt_ready, 1)
                elif kind == "gram":
                    if halves == 0:
                        dve.wait_ge(zt_ready, 1)
                    if i == 0 and t >= 2:
                        dve.wait_ge(low_in[t - 2], 16 * MOVES)
                    dve.wait_ge(gram_full, halves + 1)
                    copy_gram(nc.vector.tensor_copy, t, i, halves % 2,
                              range(SAMPLES - ACT_SAMPLES)).then_inc(gram_dve, 1)
                    halves += 1
                elif kind == "layer1" and i == 1:
                    if t:
                        dve.wait_ge(l2_full, t)
                    if t < TILES - 1:
                        dve.wait_ge(l1_full, t + 1)
                        nc.vector.tensor_scalar(h1[:], l1[:], 0.0, None, ALU.max).then_inc(h1_ready, 1)
                    else:
                        for u in range(BLOCKS):
                            dve.wait_ge(l1_full, units_ready(t, u))
                            nc.vector.tensor_scalar(h1[:, u, :], l1_block(t, u), 0.0, None,
                                                    ALU.max).then_inc(h1_ready, 1)
                elif kind == "layer2":
                    dve.wait_ge(l2_full, t + 1)
                    if t == 0:
                        dve.wait_ge(w2_in, 3 * 16)
                    else:
                        dve.wait_ge(y_ready, t)
                    nc.vector.tensor_tensor(h2[:], l2[:, 0:H2], b2_sb[:], ALU.add).then_inc(h2_sum, 1)
                    dve.wait_ge(h2_sum, t + 1)
                    nc.vector.scalar_tensor_tensor(out=h2w[:], in0=h2[:], scalar=0.0, in1=w3_sb[:], op0=ALU.max,
                                                   op1=ALU.mult, accum_out=y[:, t:t + 1]).then_inc(y_ready, 1)


def kernel(**inputs):
    import numpy as np
    import concourse.bacc as bacc
    from concourse import mybir as mb
    from concourse.bass_utils import run_bass_kernel_spmd as run

    nc = bacc.Bacc("TRN2", target_bir_lowering=False, num_devices=1)
    place_of = {0: 0, **{f + 1: 1 + i for i, f in enumerate(PLACE_FIELDS)}}
    top1 = np.asarray(inputs["W_top1"])
    w1 = np.zeros((P, CHUNKS + 1, H1), top1.dtype)
    pairs = [sorted((place_of[n], place_of[m])) for n in range(PLACES) for m in range(n + 1, PLACES)]
    for row, (n, m) in enumerate(pairs):
        if m > LOW:
            g, c = divmod(m - LOW - 1, CHUNKS)
            w1[PAD * g + n, c] = top1[row]
        elif m > SMALL:
            g, c = divmod(m - SMALL - 1, CHUNKS)
            g = QUADS - 1 - g
            w1[PAD * g + LOW_AT[g] + n, c] = top1[row]
        else:
            w1[SMALL_AT + n, m - 1] = top1[row]
    w1[BIAS_AT, CHUNKS - 1] = np.asarray(inputs["b_top1"])
    w1[:, CHUNKS] = top1[len(pairs):]
    ids = np.asarray(inputs["ids"])
    arrays = {"dense": inputs["r_dense"], "ids": ids, "ids_oh": ids[:, ONEHOT].T, "w1": w1, "w2": inputs["W_top2"],
              "b2": inputs["b_top2"], "w3": inputs["W_top3"]}
    arrays.update({f"tbl_{f}": inputs[f"tbl_{f}"] for f in range(FIELDS)})
    arrays = {n: np.ascontiguousarray(a) for n, a in arrays.items()}
    aps = {n: nc.dram_tensor(n, a.shape, mb.dt.from_np(a.dtype), kind="ExternalInput").ap() for n, a in arrays.items()}
    out = nc.dram_tensor("y_out_dram", (BATCH, 1), mb.dt.float32, kind="ExternalOutput").ap()
    dlrm_tower(nc, aps["dense"], aps["ids"], aps["ids_oh"], [aps[f"tbl_{f}"] for f in range(FIELDS)], aps["w1"],
               aps["w2"], aps["b2"], aps["w3"], out)
    r = run(nc, [arrays], core_ids=[0])
    return r.results[0]["y_out_dram"]
```

```python
from contextlib import ExitStack

import concourse.bass as bass
from concourse import mybir

P = 128
BATCH = 512
TILES = BATCH // P
D = 128
SIZES = [12500, 125000, 1250, 12500, 1000, 1000, 1000, 12500, 12500, 1250, 12500, 1250, 1000, 1250, 1250, 1250, 1000,
         12500, 1250, 12500, 12500, 1250, 1250, 1000, 1250, 1250]
FIELDS = len(SIZES)
PLACES = FIELDS + 1
PAD = 32
SAMPLES = 4
H1 = 512
H2 = 256

ONEHOT = [4, 5, 6, 12, 16, 23, 2, 9]
K_OH = len(ONEHOT)
OH_ROWS = 125
OH_CHUNKS = [SIZES[f] // OH_ROWS for f in ONEHOT]
KINDS = sorted(set(OH_CHUNKS))
MOST = max(OH_CHUNKS)
TABLES = 3
DENSE_AFTER = 4
HEADED = 2
HEAD = 3
PARTS = 3
HOTS = 8
ACT_EVERY = 4
ROWS_AFTER = {K_OH - 3: [0, 1], K_OH - 2: [2, 3, 4]}

GATHERED = [f for f in range(FIELDS) if f not in ONEHOT]
PLACE_FIELDS = ONEHOT + GATHERED
FIRST = 1 + K_OH
ROW_TILES = 2
GROUPS = [(a, min(4, PLACES - a)) for a in range(FIRST, PLACES, 4)]

CHUNKS = 3
QUADS = P // PAD
LOW = FIELDS - QUADS * CHUNKS
SMALL = LOW - QUADS * CHUNKS
HIGH_ROWS = [LOW + CHUNKS * (g + 1) for g in range(QUADS)]
LOW_ROWS = [LOW - CHUNKS * g for g in range(QUADS)]
LOW_AT = [PAD - n for n in LOW_ROWS]
SMALL_AT = LOW_AT[0] - SMALL
MOVES = QUADS + 1
SHARED_MOVES = 2
BLOCKS = H1 // P
BIAS_AT = PAD + HIGH_ROWS[1]
HALVES = 4
QH = P // SAMPLES // HALVES
ACT_SAMPLES = 2
WARM_UP = 16


LOW_PARTS = {(i, OH_CHUNKS[i] // 2 + 1): (i + 1, 0, OH_CHUNKS[i + 1]) for i in range(1, K_OH - 1)}
LOW_PARTS.update({(0, 1): (0, 0, HEAD), (0, 4): (0, HEAD, OH_CHUNKS[0]), (0, 5): (1, 0, HEAD),
                  (1, 1): (1, HEAD, OH_CHUNKS[1])})


def timeline():
    steps = []
    for i in range(K_OH):
        steps.append(("onehot", 0, i))
        if i == DENSE_AFTER:
            steps.append(("dense", 0, 0))
        steps += [("rows", 0, g) for g in ROWS_AFTER.get(i, [])]
    steps += [("rows", 1, 0), ("rows", 1, 1), ("gram", 0, 0), ("gram", 0, 1), ("rows", 1, 2), ("gram", 0, 2),
              ("rows", 1, 3), ("rows", 1, 4), ("gram", 0, 3)]
    steps += [("gram", 1, 0), ("rows", 2, 0), ("gram", 1, 1), ("rows", 2, 1), ("gram", 1, 2), ("layer1", 0, 0),
              ("layer1", 0, 1), ("rows", 2, 2), ("gram", 1, 3), ("rows", 2, 3), ("rows", 2, 4), ("layer2", 0, 0)]
    steps += [("gram", 2, 0), ("gram", 2, 1), ("rows", 3, 0), ("gram", 2, 2), ("gram", 2, 3), ("layer1", 1, 0),
              ("layer1", 1, 1), ("rows", 3, 1), ("rows", 3, 2), ("layer2", 1, 0), ("rows", 3, 3), ("layer1", 2, 0),
              ("rows", 3, 4)]
    steps += [("gram", 3, h) for h in range(HALVES)]
    steps += [("layer1", 2, 1), ("layer1", 3, 0), ("layer2", 2, 0), ("layer1", 3, 1), ("layer2", 3, 0)]
    return steps


STEPS = timeline()


def banks_filled(step):
    return sum(kind in ("dense", "rows") for kind, _, _ in STEPS[:STEPS.index(step) + 1])


def first_hot(i):
    return sum(OH_CHUNKS[:i])


def split_parts(i, c):
    return i + min(i, HEADED) + (1 if i >= HEADED or c < HEAD else 2)


def units_ready(t, u):
    return t + 1 + (u if t == TILES - 1 else 0)


def by_scalar(k):
    return k % ACT_EVERY == ACT_EVERY - 1


def hots_made(k, scalar):
    return sum(by_scalar(x) == scalar for x in range(k + 1))


def dlrm_tower(nc, dense, ids, ids_oh, tbls, w1, w2, b2, w3, out):
    f32, f32r, i32 = mybir.dt.float32, mybir.dt.float32r, mybir.dt.int32
    ALU, ACT = mybir.AluOpType, mybir.ActivationFunctionType
    with ExitStack() as ctx:
        def sb(name, shape, dt=f32):
            return ctx.enter_context(nc.sbuf_tensor(name, shape, dt))

        def pb(name, shape):
            return ctx.enter_context(nc.psum_tensor(name, shape, f32))

        def sem(name):
            return ctx.enter_context(nc.semaphore(name))

        idx = sb("idx", [P, TILES, FIELDS], i32)
        dense_sb = sb("dense_sb", [P, TILES, D])
        rows = sb("rows", [P, ROW_TILES, len(GATHERED), D])
        XT = sb("XT", [P, BATCH, PAD])
        Zt = sb("Zt", [P, CHUNKS, BATCH])
        Zlow = sb("Zlow", [LOW, 2, LOW, P])
        w1_sb = sb("w1_sb", [P, CHUNKS + 1, H1])
        w2_sb = sb("w2_sb", [P, BLOCKS, H2])
        b2_sb = sb("b2_sb", [P, H2])
        w3_sb = sb("w3_sb", [P, H2])
        ident = sb("ident", [P, P])
        h1 = sb("h1", [P, BLOCKS, P])
        h2 = sb("h2", [P, H2])
        h2w = sb("h2w", [P, H2])
        y = sb("y", [P, TILES])
        ids_bc = sb("ids_bc", [OH_ROWS, TABLES, BATCH], i32)
        rownum_i = sb("rownum_i", [OH_ROWS, len(KINDS), MOST], i32)
        rownum = sb("rownum", [OH_ROWS, len(KINDS), MOST])
        minus_row = sb("minus_row", [OH_ROWS, len(KINDS), MOST])
        table = sb("table", [OH_ROWS, TABLES, MOST * D])
        t_hi = sb("t_hi", [OH_ROWS, PARTS, MOST * D], f32r)
        t_lo = sb("t_lo", [OH_ROWS, PARTS, MOST * D], f32r)
        hot = sb("hot", [OH_ROWS, HOTS, BATCH], f32r)
        apart = sb("apart", [OH_ROWS, 2, BATCH])
        tp = pb("tp", [P, 2, BATCH])
        gr = pb("gr", [P, 2, QH, SAMPLES, PAD])
        l1 = pb("l1", [P, BLOCKS, P])
        l2 = pb("l2", [P, 2 * H2])

        idx_in, dense_in, w1_in, w2_in = sem("idx_in"), sem("dense_in"), sem("w1_in"), sem("w2_in")
        ids_in = [sem(f"ids_in{i}") for i in range(K_OH)]
        tail_in = [sem(f"tail_in{i}") for i in range(HEADED)]
        table_in = [sem(f"table_in{i}") for i in range(K_OH)]
        rows_in = [[sem(f"rows_in{t}_{g}") for g in range(len(GROUPS))] for t in range(TILES)]
        low_in = [sem(f"low_in{t}") for t in range(TILES)]
        idx_rest_in = sem("idx_rest_in")
        low_in_pool, y_out = sem("low_in_pool"), sem("y_out")
        ident_zero, ident_ready, xt_ready, zt_ready = (
            sem("ident_zero"), sem("ident_ready"), sem("xt_ready"), sem("zt_ready"))
        iota_ready, rownum_ready = sem("iota_ready"), sem("rownum_ready")
        hi_ready, lo_ready, apart_ready = sem("hi_ready"), sem("lo_ready"), sem("apart_ready")
        hot_dve, hot_act, hot_used = sem("hot_dve"), sem("hot_act"), sem("hot_used")
        lookup_copied, tp_full, tp_empty = sem("lookup_copied"), sem("tp_full"), sem("tp_empty")
        gram_full, gram_dve, gram_act = sem("gram_full"), sem("gram_dve"), sem("gram_act")
        low_dve, low_act = sem("low_dve"), sem("low_act")
        l1_full, h1_ready, l2_full = sem("l1_full"), sem("h1_ready"), sem("l2_full")
        h2_sum, y_ready = sem("h2_sum"), sem("y_ready")

        def lookup_bank(i):
            return l2[:] if i % 2 else l1[:].rearrange("p u b -> p (u b)")

        def l1_block(t, u):
            if t < TILES - 1:
                return l1[:, u, :]
            return gr[:].rearrange("p h q s n -> p (h q s n)")[:, u * 2 * H2:u * 2 * H2 + P]

        block = ctx.enter_context(nc.Block())

        def low_stars(queue, t, quadrants, moved):
            queue.wait_ge(low_dve, HALVES * (t + 1))
            queue.wait_ge(low_act, HALVES * (t + 1))
            queue.wait_ge(zt_ready, 1)
            for g in quadrants:
                n = LOW_ROWS[g]
                queue.dma_start(Zt[PAD * g + LOW_AT[g]:PAD * (g + 1), :, t * P:(t + 1) * P],
                                Zlow[0:n, t % 2, n - CHUNKS:n, :]).then_inc(moved, 16)

        @block.sync
        def _(sp):
            def table_ids(i):
                if i >= TABLES:
                    sp.wait_ge(hot_used, first_hot(i - TABLES + 1))
                sp.dma_start(ids_bc[:, i % TABLES, :],
                             ids_oh[i:i + 1, :].broadcast_to((OH_ROWS, BATCH))).then_inc(ids_in[i], 16)

            sp.dma_start(idx[:, 0, :], ids[0:P, :]).then_inc(idx_in, 16)
            table_ids(0)
            for i, f in enumerate(ONEHOT):
                n = OH_CHUNKS[i]
                if i >= TABLES:
                    sp.wait_ge(lo_ready, split_parts(i - TABLES, MOST))
                source = tbls[f].rearrange("(p c) d -> p (c d)", c=n)
                for part, (c0, c1) in enumerate([(0, HEAD), (HEAD, n)] if i < HEADED else [(0, n)]):
                    sp.dma_start(table[:, i % TABLES, c0 * D:c1 * D],
                                 source[:, c0 * D:c1 * D]).then_inc(table_in[i] if part == 0 else tail_in[i], 16)
                if i > 0:
                    table_ids(i)
                if i == HEADED - 1:
                    sp.dma_start(idx[:, 1:TILES, :],
                                 ids[P:BATCH, :].rearrange("(t p) f -> p t f", p=P)).then_inc(idx_rest_in, 16)
                if i == DENSE_AFTER:
                    sp.dma_start(dense_sb[:], dense.rearrange("(t p) d -> p t d", p=P)).then_inc(dense_in, 16)
            sp.dma_start(w1_sb[:], w1).then_inc(w1_in, 16)
            sp.dma_start(w2_sb[:], w2.rearrange("(j p) k -> p j k", p=P)).then_inc(w2_in, 16)
            sp.dma_start(b2_sb[:], b2.rearrange("(o k) -> o k", o=1).broadcast_to((P, H2))).then_inc(w2_in, 16)
            sp.dma_start(w3_sb[:], w3.rearrange("k o -> o k").broadcast_to((P, H2))).then_inc(w2_in, 16)

            def result(t):
                sp.wait_ge(y_ready, t + 1)
                with nc.allow_non_contiguous_dma(reason="one value per sample"):
                    sp.dma_start(out[t * P:(t + 1) * P, :], y[:, t:t + 1]).then_inc(y_out, 16)

            for t in range(TILES):
                low_stars(sp, t, range(QUADS - (SHARED_MOVES if t == TILES - 1 else 0)), low_in[t])
                sp.wait_ge(gram_dve, HALVES * (t + 1))
                sp.wait_ge(gram_act, HALVES * (t + 1))
                sp.dma_start(Zt[SMALL_AT:SMALL_AT + SMALL, 0:SMALL, t * P:(t + 1) * P],
                             Zlow[0:SMALL, t % 2, 0:SMALL, :]).then_inc(low_in[t], 16)
                if t:
                    result(t - 1)
            result(TILES - 1)
            sp.wait_ge(y_out, 16 * TILES)

        @block.gpsimd
        def _(pool):
            nc.gpsimd.memset(ident[:], 0.0).then_inc(ident_zero, 1)
            for v, n in enumerate(KINDS):
                nc.gpsimd.iota(rownum_i[:, v, :], pattern=[[1, MOST]], base=0,
                               channel_multiplier=n).then_inc(iota_ready, 1)
            pool.wait_ge(ident_zero, 1)
            nc.gpsimd.affine_select(out=ident[:], in_=ident[:], compare_op=ALU.not_equal, fill=1.0, base=0,
                                    pattern=[[-1, P]], channel_multiplier=1).then_inc(ident_ready, 1)
            for t in range(TILES):
                pool.wait_ge(idx_rest_in if t else idx_in, 16)
                for g, (a, n) in enumerate(GROUPS):
                    if t >= ROW_TILES:
                        pool.wait_ge(tp_full, banks_filled(("rows", t - ROW_TILES, g)))
                    for place in range(a, a + n):
                        f = PLACE_FIELDS[place - 1]
                        nc.gpsimd.indirect_dma_start(
                            rows[:, t % ROW_TILES, place - FIRST, :], None, tbls[f],
                            bass.IndirectOffsetOnAxis(ap=idx[:, t, f:f + 1], axis=0)).then_inc(rows_in[t][g], 16)
            low_stars(nc.gpsimd, TILES - 1, range(QUADS - SHARED_MOVES, QUADS), low_in_pool)

        @block.tensor
        def _(pe):
            banks, halves = 0, 0

            def from_dense(t, u):
                nc.tensor.matmul(l1_block(t, u), w1_sb[:, CHUNKS, u * P:(u + 1) * P], XT[:, t * P:(t + 1) * P, 0],
                                 start=True, stop=False)

            def from_pairs(t, u):
                for c in range(CHUNKS):
                    last = nc.tensor.matmul(l1_block(t, u), w1_sb[:, c, u * P:(u + 1) * P],
                                            Zt[:, c, t * P:(t + 1) * P], start=False, stop=c == CHUNKS - 1)
                return last

            pe.wait_ge(ident_ready, 1)
            for _ in range(WARM_UP):
                nc.tensor.transpose(l2[:, 0:P], ident[:], ident[:])
            for kind, t, i in STEPS:
                tile = slice(t * P, (t + 1) * P)
                bank = banks % 2
                if kind in ("dense", "rows"):
                    if banks >= 2:
                        pe.wait_ge(tp_empty, banks - 1)
                    banks += 1
                if kind == "dense":
                    pe.wait_ge(dense_in, 16)
                    for j in range(TILES):
                        last = nc.tensor.transpose(tp[:, bank, j * P:(j + 1) * P], dense_sb[:, j, :], ident[:])
                    last.then_inc(tp_full, 1)
                elif kind == "rows":
                    a, n = GROUPS[i]
                    pe.wait_ge(rows_in[t][i], 16 * n)
                    for j in range(n):
                        last = nc.tensor.transpose(tp[:, bank, j * P:(j + 1) * P],
                                                   rows[:, t % ROW_TILES, a + j - FIRST, :], ident[:])
                    last.then_inc(tp_full, 1)
                elif kind == "onehot":
                    n = OH_CHUNKS[i]
                    if i >= 2:
                        pe.wait_ge(lookup_copied, i - 1)
                    for c in range(n):
                        k = first_hot(i) + c
                        pe.wait_ge(hi_ready, split_parts(i, c))
                        pe.wait_ge(lo_ready, split_parts(i, c))
                        pe.wait_ge(hot_act if by_scalar(k) else hot_dve, hots_made(k, by_scalar(k)))
                        nc.tensor.matmul(lookup_bank(i), t_hi[:, i % PARTS, c * D:(c + 1) * D], hot[:, k % HOTS, :],
                                         start=c == 0, stop=False)
                        nc.tensor.matmul(lookup_bank(i), t_lo[:, i % PARTS, c * D:(c + 1) * D], hot[:, k % HOTS, :],
                                         start=False, stop=c == n - 1).then_inc(hot_used, 1)
                elif kind == "gram":
                    pe.wait_ge(tp_empty, banks_filled(("rows", t, len(GROUPS) - 1)))
                    if halves == 0:
                        pe.wait_ge(lookup_copied, K_OH)
                        pe.wait_ge(xt_ready, 1)
                    if halves >= 2:
                        pe.wait_ge(gram_dve, halves - 1)
                        pe.wait_ge(gram_act, halves - 1)
                    for q in range(QH):
                        b = t * P + SAMPLES * (i * QH + q)
                        last = nc.tensor.matmul(gr[:, halves % 2, q, :, 0:FIELDS],
                                                XT[:, b:b + SAMPLES, :].rearrange("d s n -> d (s n)"),
                                                XT[:, b:b + SAMPLES, 1:PLACES], start=True, stop=True)
                    last.then_inc(gram_full, 1)
                    halves += 1
                elif kind == "layer1" and t == TILES - 1 and i == 0:
                    pe.wait_ge(gram_dve, HALVES * TILES)
                    pe.wait_ge(gram_act, HALVES * TILES)
                    for u in range(BLOCKS):
                        from_dense(t, u)
                elif kind == "layer1" and t == TILES - 1:
                    pe.wait_ge(low_in[t], 16 * (MOVES - SHARED_MOVES))
                    pe.wait_ge(low_in_pool, 16 * SHARED_MOVES)
                    for u in range(BLOCKS):
                        from_pairs(t, u).then_inc(l1_full, 1)
                elif kind == "layer1":
                    if i == 0:
                        if t == 0:
                            pe.wait_ge(w1_in, 16)
                        else:
                            pe.wait_ge(h1_ready, t)
                        pe.wait_ge(gram_dve, HALVES * (t + 1))
                        pe.wait_ge(gram_act, HALVES * (t + 1))
                        pe.wait_ge(low_in[t], 16 * MOVES)
                    for u in range(i * BLOCKS // 2, (i + 1) * BLOCKS // 2):
                        from_dense(t, u)
                        last = from_pairs(t, u)
                    if i == 1:
                        last.then_inc(l1_full, 1)
                elif kind == "layer2":
                    if t == 0:
                        pe.wait_ge(w2_in, 3 * 16)
                    else:
                        pe.wait_ge(h2_sum, t)
                    for u in range(BLOCKS):
                        pe.wait_ge(h1_ready, units_ready(t, u))
                        last = nc.tensor.matmul(l2[:, 0:H2], h1[:, u, :], w2_sb[:, u, :], start=u == 0,
                                                stop=u == BLOCKS - 1)
                    last.then_inc(l2_full, 1)

        def copy_gram(copy, t, h, half, samples, low_copied):
            def columns(s):
                first = h * QH * SAMPLES + s
                return first, first + (QH - 1) * SAMPLES + 1

            for s in samples:
                first, end = columns(s)
                last = copy(Zlow[:, t % 2, :, first:end:SAMPLES].rearrange("n m q -> n q m"),
                            gr[PAD * s:PAD * s + LOW, half, :, s, 0:LOW])
            last.then_inc(low_copied, 1)
            for s in samples:
                first, end = columns(s)
                for g, n in enumerate(HIGH_ROWS):
                    last = copy(
                        Zt[PAD * g:PAD * g + n, :, t * P + first:t * P + end:SAMPLES].rearrange("n c q -> n q c"),
                        gr[PAD * s:PAD * s + n, half, :, s, n - CHUNKS:n])
            return last

        @block.scalar
        def _(act):
            banks, halves = 0, 0

            def high_part(i, c0, c1):
                act.wait_ge(tail_in[i] if i < HEADED and c0 else table_in[i], 16)
                if i >= PARTS:
                    act.wait_ge(hot_used, first_hot(i - PARTS + 1))
                nc.scalar.copy(t_hi[:, i % PARTS, c0 * D:c1 * D],
                               table[:, i % TABLES, c0 * D:c1 * D]).then_inc(hi_ready, 1)

            mine = [k for k in range(first_hot(K_OH)) if by_scalar(k)]
            table_of = [i for i in range(K_OH) for _ in range(OH_CHUNKS[i])]

            def mine_in(i):
                return [k for k in mine if table_of[k] == i]

            def distance(j):
                i = table_of[mine[j]]
                act.wait_ge(ids_in[i], 16)
                act.wait_ge(rownum_ready, 2)
                if j >= 2:
                    act.wait_ge(hot_act, j - 1)
                c = mine[j] - first_hot(i)
                nc.scalar.activation(apart[:, j % 2, :], ids_bc[:, i % TABLES, :], ACT.Abs,
                                     bias=minus_row[:, KINDS.index(OH_CHUNKS[i]), c:c + 1]).then_inc(apart_ready, 1)

            def one_hot(k):
                j = mine.index(k)
                act.wait_ge(apart_ready, j + 1)
                if k >= HOTS:
                    act.wait_ge(hot_used, k - HOTS + 1)
                nc.scalar.activation(hot[:, k % HOTS, :], apart[:, j % 2, :], ACT.Relu, bias=1.0,
                                     scale=-1.0).then_inc(hot_act, 1)
                if 0 < j < len(mine) - 1:
                    distance(j + 1)

            high_part(0, 0, HEAD)
            distance(0)
            high_part(0, HEAD, OH_CHUNKS[0])
            one_hot(mine_in(0)[0])
            high_part(1, 0, HEAD)
            distance(1)
            high_part(1, HEAD, OH_CHUNKS[1])
            for kind, t, i in STEPS:
                if kind == "onehot":
                    for k in mine_in(i)[1:]:
                        one_hot(k)
                    if i + 2 < K_OH:
                        high_part(i + 2, 0, OH_CHUNKS[i + 2])
                    if i + 1 < K_OH:
                        one_hot(mine_in(i + 1)[0])
                    act.wait_ge(hot_used, first_hot(i + 1))
                    nc.scalar.copy(XT[:, :, 1 + i], lookup_bank(i)).then_inc(lookup_copied, 1)
                elif kind == "gram":
                    if halves == 0:
                        act.wait_ge(zt_ready, 1)
                    if i == 0 and t >= 2:
                        act.wait_ge(low_in[t - 2], 16 * MOVES)
                    act.wait_ge(gram_full, halves + 1)
                    copy_gram(nc.scalar.copy, t, i, halves % 2,
                              range(SAMPLES - ACT_SAMPLES, SAMPLES), low_act).then_inc(gram_act, 1)
                    halves += 1
                elif kind in ("dense", "rows"):
                    act.wait_ge(tp_full, banks_filled((kind, t, i)))
                    if kind == "dense":
                        nc.scalar.copy(XT[:, :, 0], tp[:, banks % 2, :]).then_inc(tp_empty, 1)
                    else:
                        a, n = GROUPS[i]
                        nc.scalar.copy(
                            XT[:, t * P:(t + 1) * P, a:a + n],
                            tp[:, banks % 2, 0:n * P].rearrange("p (n b) -> p b n", n=n)).then_inc(tp_empty, 1)
                    banks += 1

        @block.vector
        def _(dve):
            halves = 0
            nc.vector.memset(Zt[:], 1.0).then_inc(zt_ready, 1)
            dve.wait_ge(iota_ready, len(KINDS))
            nc.vector.tensor_copy(rownum[:], rownum_i[:]).then_inc(rownum_ready, 1)
            nc.vector.tensor_scalar(minus_row[:], rownum_i[:], -1.0, None, ALU.mult).then_inc(rownum_ready, 1)
            dve.wait_ge(rownum_ready, 2)

            def low_part(i, c0, c1):
                dve.wait_ge(hi_ready, split_parts(i, c0))
                if i >= PARTS:
                    dve.wait_ge(hot_used, first_hot(i - PARTS + 1))
                nc.vector.tensor_tensor(t_lo[:, i % PARTS, c0 * D:c1 * D], table[:, i % TABLES, c0 * D:c1 * D],
                                        t_hi[:, i % PARTS, c0 * D:c1 * D].bitcast(f32),
                                        ALU.subtract).then_inc(lo_ready, 1)

            for kind, t, i in STEPS:
                if kind == "onehot":
                    dve.wait_ge(ids_in[i], 16)
                    for c in range(OH_CHUNKS[i]):
                        if (i, c) in LOW_PARTS:
                            low_part(*LOW_PARTS[i, c])
                        k = first_hot(i) + c
                        if not by_scalar(k):
                            if k >= HOTS:
                                dve.wait_ge(hot_used, k - HOTS + 1)
                            nc.vector.tensor_scalar(hot[:, k % HOTS, :], ids_bc[:, i % TABLES, :],
                                                    rownum[:, KINDS.index(OH_CHUNKS[i]), c:c + 1], None,
                                                    ALU.is_equal).then_inc(hot_dve, 1)
                    if i == K_OH - 1:
                        nc.vector.memset(XT[:, :, PLACES:PAD], 0.0).then_inc(xt_ready, 1)
                elif kind == "gram":
                    if halves == 0:
                        dve.wait_ge(zt_ready, 1)
                    if i == 0 and t >= 2:
                        dve.wait_ge(low_in[t - 2], 16 * MOVES)
                    dve.wait_ge(gram_full, halves + 1)
                    copy_gram(nc.vector.tensor_copy, t, i, halves % 2,
                              range(SAMPLES - ACT_SAMPLES), low_dve).then_inc(gram_dve, 1)
                    halves += 1
                elif kind == "layer1" and i == 1:
                    if t:
                        dve.wait_ge(l2_full, t)
                    if t < TILES - 1:
                        dve.wait_ge(l1_full, t + 1)
                        nc.vector.tensor_scalar(h1[:], l1[:], 0.0, None, ALU.max).then_inc(h1_ready, 1)
                    else:
                        for u in range(BLOCKS):
                            dve.wait_ge(l1_full, units_ready(t, u))
                            nc.vector.tensor_scalar(h1[:, u, :], l1_block(t, u), 0.0, None,
                                                    ALU.max).then_inc(h1_ready, 1)
                elif kind == "layer2":
                    dve.wait_ge(l2_full, t + 1)
                    if t == 0:
                        dve.wait_ge(w2_in, 3 * 16)
                    else:
                        dve.wait_ge(y_ready, t)
                    nc.vector.tensor_tensor(h2[:], l2[:, 0:H2], b2_sb[:], ALU.add).then_inc(h2_sum, 1)
                    dve.wait_ge(h2_sum, t + 1)
                    nc.vector.scalar_tensor_tensor(out=h2w[:], in0=h2[:], scalar=0.0, in1=w3_sb[:], op0=ALU.max,
                                                   op1=ALU.mult, accum_out=y[:, t:t + 1]).then_inc(y_ready, 1)


def kernel(**inputs):
    import numpy as np
    import concourse.bacc as bacc
    from concourse import mybir as mb
    from concourse.bass_utils import run_bass_kernel_spmd as run

    nc = bacc.Bacc("TRN2", target_bir_lowering=False, num_devices=1)
    place_of = {0: 0, **{f + 1: 1 + i for i, f in enumerate(PLACE_FIELDS)}}
    top1 = np.asarray(inputs["W_top1"])
    w1 = np.zeros((P, CHUNKS + 1, H1), top1.dtype)
    pairs = [sorted((place_of[n], place_of[m])) for n in range(PLACES) for m in range(n + 1, PLACES)]
    for row, (n, m) in enumerate(pairs):
        if m > LOW:
            g, c = divmod(m - LOW - 1, CHUNKS)
            w1[PAD * g + n, c] = top1[row]
        elif m > SMALL:
            g, c = divmod(m - SMALL - 1, CHUNKS)
            g = QUADS - 1 - g
            w1[PAD * g + LOW_AT[g] + n, c] = top1[row]
        else:
            w1[SMALL_AT + n, m - 1] = top1[row]
    w1[BIAS_AT, CHUNKS - 1] = np.asarray(inputs["b_top1"])
    w1[:, CHUNKS] = top1[len(pairs):]
    ids = np.asarray(inputs["ids"])
    arrays = {"dense": inputs["r_dense"], "ids": ids, "ids_oh": ids[:, ONEHOT].T, "w1": w1, "w2": inputs["W_top2"],
              "b2": inputs["b_top2"], "w3": inputs["W_top3"]}
    arrays.update({f"tbl_{f}": inputs[f"tbl_{f}"] for f in range(FIELDS)})
    arrays = {n: np.ascontiguousarray(a) for n, a in arrays.items()}
    aps = {n: nc.dram_tensor(n, a.shape, mb.dt.from_np(a.dtype), kind="ExternalInput").ap() for n, a in arrays.items()}
    out = nc.dram_tensor("y_out_dram", (BATCH, 1), mb.dt.float32, kind="ExternalOutput").ap()
    dlrm_tower(nc, aps["dense"], aps["ids"], aps["ids_oh"], [aps[f"tbl_{f}"] for f in range(FIELDS)], aps["w1"],
               aps["w2"], aps["b2"], aps["w3"], out)
    r = run(nc, [arrays], core_ids=[0])
    return r.results[0]["y_out_dram"]
```
